# Optimizing a Trainium2 kernel written in Bass

```python
import numpy as np
import jax
import jax.numpy as jnp

def _softmax(x, axis=-1):
    return jax.nn.softmax(x, axis=axis)

def _gelu(x):
    return jax.nn.gelu(x, approximate=True)

def _silu(x):
    return jax.nn.silu(x)

def _sigmoid(x):
    return jax.nn.sigmoid(x)

def _layernorm(x, axis=-1, eps=1e-05):
    m = jnp.mean(x, axis=axis, keepdims=True)
    v = jnp.var(x, axis=axis, keepdims=True)
    return (x - m) / jnp.sqrt(v + eps)

def _scatter_add(tgt, idx, src, axis=0):
    return tgt.at[idx].add(src)

def _segment_sum(src, seg, n):
    return jax.ops.segment_sum(src, seg, n)
kernel_name = 'mk_gnn_ffn_d2_gnn_r32_e23780'

def setup_inputs(seed: int=0):
    np.random.seed(seed)
    _w = jnp.asarray

    def _rec_inputs():
        import jax
        import jax.numpy as jnp
        _gk = jax.random.key(seed)
        x = -5.39e-05 + 0.9998 * jax.random.normal(jax.random.fold_in(_gk, 1), (3125, 256), jnp.float32)
        src = jax.random.randint(jax.random.fold_in(_gk, 2), (50000,), 0, 3125, jnp.int32)
        dst = jax.random.randint(jax.random.fold_in(_gk, 3), (50000,), 0, 3125, jnp.int32)
        _o = jnp.argsort(dst, stable=True)
        src = src[_o]
        dst = dst[_o]
        return (x, src, dst)
    x, src, dst = _rec_inputs()

    def _L0_gnn_setup():
        import jax, jax.numpy as jnp
        import numpy as np
        NUM_NODES = 3125
        IN_CH = 256
        HIDDEN = 128
        OUT_CH = 256
        NUM_EDGES = 100000

        def gcn_conv(x, W, b, src, dst, num_nodes):
            h = x @ W
            loop = jnp.arange(num_nodes, dtype=src.dtype)
            s = jnp.concatenate([src, loop])
            d = jnp.concatenate([dst, loop])
            deg = jax.ops.segment_sum(jnp.ones_like(d, dtype=h.dtype), d, num_segments=num_nodes)
            dinv = jnp.where(deg > 0, jax.lax.rsqrt(deg), 0.0)
            norm = dinv[s] * dinv[d]
            msg = h[s] * norm[:, None]
            out = jax.ops.segment_sum(msg, d, num_segments=num_nodes)
            return out + b
        key = jax.random.key(seed)
        k1, k2, k3, k4 = jax.random.split(key, 4)
        edge_index = jax.random.randint(k1, (2, NUM_EDGES), 0, NUM_NODES, dtype=jnp.int64)
        node_features = jax.random.normal(k2, (NUM_NODES, IN_CH), dtype=jnp.float32)
        W1 = jax.random.normal(k3, (IN_CH, HIDDEN), dtype=jnp.float32) * (1.0 / np.sqrt(IN_CH))
        b1 = jnp.zeros((HIDDEN,), dtype=jnp.float32)
        W2 = jax.random.normal(k4, (HIDDEN, OUT_CH), dtype=jnp.float32) * (1.0 / np.sqrt(HIDDEN))
        b2 = jnp.zeros((OUT_CH,), dtype=jnp.float32)
        return {'node_features': node_features, 'W1': W1, 'b1': b1, 'W2': W2, 'b2': b2, 'edge_index': edge_index}
    _L0_gnn_all = _L0_gnn_setup()
    _L0_gnn_in = {k: v for k, v in _L0_gnn_all.items() if k in ('W1', 'b1', 'W2', 'b2')}
    del _L0_gnn_all

    def _L0_ffn_setup():
        import math
        import jax, jax.numpy as jnp
        import numpy as np
        CAPACITY_FACTOR = 1.25
        TOP_K = 2
        LN_EPS = 1e-05

        def _layer_norm(x, gamma, beta):
            mu = jnp.mean(x, axis=-1, keepdims=True)
            var = jnp.var(x, axis=-1, keepdims=True)
            return (x - mu) * jax.lax.rsqrt(var + LN_EPS) * gamma + beta
        key = jax.random.key(seed)
        ks = jax.random.split(key, 4)
        B, S, D, F, E = (8, 128, 256, 512, 8)
        x = jax.random.normal(ks[0], (B, S, D), dtype=jnp.float32)
        Wr = jax.random.normal(ks[1], (D, E), dtype=jnp.float32) / np.sqrt(D)
        br = jnp.zeros((E,), jnp.float32)
        W1 = jax.random.normal(ks[2], (E, D, F), dtype=jnp.float32) / np.sqrt(D)
        b1 = jnp.zeros((E, F), jnp.float32)
        W2 = jax.random.normal(ks[3], (E, F, D), dtype=jnp.float32) / np.sqrt(F)
        b2 = jnp.zeros((E, D), jnp.float32)
        gamma = jnp.ones((D,), jnp.float32)
        beta = jnp.zeros((D,), jnp.float32)
        return {'x': x, 'Wr': Wr, 'br': br, 'W1': W1, 'b1': b1, 'W2': W2, 'b2': b2, 'gamma': gamma, 'beta': beta}
    _L0_ffn_all = _L0_ffn_setup()
    _L0_ffn_in = {k: v for k, v in _L0_ffn_all.items() if k in ('Wr', 'br', 'W1', 'b1', 'W2', 'b2', 'gamma', 'beta')}
    del _L0_ffn_all

    def _L1_gnn_setup():
        import jax, jax.numpy as jnp
        import numpy as np
        N_NODES = 50000
        N_EDGES = 25000
        IN_FEAT = 256
        HEADS = 4
        OUT_FEAT = 64
        NEG_SLOPE = 0.2
        key = jax.random.key(seed)
        k1, k2, k3, k4, k5, k6 = jax.random.split(key, 6)
        x = jax.random.normal(k1, (N_NODES, IN_FEAT), dtype=jnp.float32)
        edge_index = jax.random.randint(k2, (2, N_EDGES), 0, N_NODES, dtype=jnp.int64)
        scale = 1.0 / np.sqrt(IN_FEAT)
        W = jax.random.normal(k3, (IN_FEAT, HEADS * OUT_FEAT), dtype=jnp.float32) * scale
        att_src = jax.random.normal(k4, (HEADS, OUT_FEAT), dtype=jnp.float32) * scale
        att_dst = jax.random.normal(k5, (HEADS, OUT_FEAT), dtype=jnp.float32) * scale
        bias = jax.random.normal(k6, (HEADS * OUT_FEAT,), dtype=jnp.float32) * 0.01
        return {'x': x, 'edge_index': edge_index, 'W': W, 'att_src': att_src, 'att_dst': att_dst, 'bias': bias}
    _L1_gnn_all = _L1_gnn_setup()
    _L1_gnn_in = {k: v for k, v in _L1_gnn_all.items() if k in ('W', 'att_src', 'att_dst', 'bias')}
    del _L1_gnn_all

    def _L1_ffn_setup():
        import jax, jax.numpy as jnp
        import numpy as np
        B, T, D, H, E = (16, 128, 256, 512, 8)
        key = jax.random.key(seed)
        ks = jax.random.split(key, 5)
        x = jax.random.normal(ks[0], (B, T, D), dtype=jnp.float32)
        gate_w = jax.random.normal(ks[1], (D, E), dtype=jnp.float32) * 0.02
        gate_b = jnp.zeros((E,), dtype=jnp.float32)
        W1 = jax.random.normal(ks[2], (E, D, H), dtype=jnp.float32) * 0.02
        b1 = jnp.zeros((E, H), dtype=jnp.float32)
        W2 = jax.random.normal(ks[3], (E, H, D), dtype=jnp.float32) * 0.02
        b2 = jnp.zeros((E, D), dtype=jnp.float32)
        return {'x': x, 'gate_w': gate_w, 'gate_b': gate_b, 'W1': W1, 'b1': b1, 'W2': W2, 'b2': b2}
    _L1_ffn_all = _L1_ffn_setup()
    _L1_ffn_in = {k: v for k, v in _L1_ffn_all.items() if k in ('gate_w', 'gate_b', 'W1', 'b1', 'W2', 'b2')}
    del _L1_ffn_all
    return {'x': x, 'src': src, 'dst': dst, 'L0_gnn_W1': _L0_gnn_in['W1'], 'L0_gnn_b1': _L0_gnn_in['b1'], 'L0_gnn_W2': _L0_gnn_in['W2'], 'L0_gnn_b2': _L0_gnn_in['b2'], 'L0_ffn_Wr': _L0_ffn_in['Wr'], 'L0_ffn_br': _L0_ffn_in['br'], 'L0_ffn_W1': _L0_ffn_in['W1'], 'L0_ffn_b1': _L0_ffn_in['b1'], 'L0_ffn_W2': _L0_ffn_in['W2'], 'L0_ffn_b2': _L0_ffn_in['b2'], 'L0_ffn_gamma': _L0_ffn_in['gamma'], 'L0_ffn_beta': _L0_ffn_in['beta'], 'L1_gnn_W': _L1_gnn_in['W'], 'L1_gnn_att_src': _L1_gnn_in['att_src'], 'L1_gnn_att_dst': _L1_gnn_in['att_dst'], 'L1_gnn_bias': _L1_gnn_in['bias'], 'L1_ffn_gate_w': _L1_ffn_in['gate_w'], 'L1_ffn_gate_b': _L1_ffn_in['gate_b'], 'L1_ffn_W1': _L1_ffn_in['W1'], 'L1_ffn_b1': _L1_ffn_in['b1'], 'L1_ffn_W2': _L1_ffn_in['W2'], 'L1_ffn_b2': _L1_ffn_in['b2']}

def reference(x, src, dst, L0_gnn_W1, L0_gnn_b1, L0_gnn_W2, L0_gnn_b2, L0_ffn_Wr, L0_ffn_br, L0_ffn_W1, L0_ffn_b1, L0_ffn_W2, L0_ffn_b2, L0_ffn_gamma, L0_ffn_beta, L1_gnn_W, L1_gnn_att_src, L1_gnn_att_dst, L1_gnn_bias, L1_ffn_gate_w, L1_ffn_gate_b, L1_ffn_W1, L1_ffn_b1, L1_ffn_W2, L1_ffn_b2):
    import jax
    import jax.numpy as jnp

    def _L0_gnn_ref(node_features, W1, b1, W2, b2, edge_index):
        import jax, jax.numpy as jnp
        import numpy as np
        NUM_NODES = 3125
        IN_CH = 256
        HIDDEN = 128
        OUT_CH = 256
        NUM_EDGES = 100000

        def gcn_conv(x, W, b, src, dst, num_nodes):
            h = x @ W
            loop = jnp.arange(num_nodes, dtype=src.dtype)
            s = jnp.concatenate([src, loop])
            d = jnp.concatenate([dst, loop])
            deg = jax.ops.segment_sum(jnp.ones_like(d, dtype=h.dtype), d, num_segments=num_nodes)
            dinv = jnp.where(deg > 0, jax.lax.rsqrt(deg), 0.0)
            norm = dinv[s] * dinv[d]
            msg = h[s] * norm[:, None]
            out = jax.ops.segment_sum(msg, d, num_segments=num_nodes)
            return out + b
        src, dst = (edge_index[0], edge_index[1])
        x = gcn_conv(node_features, W1, b1, src, dst, NUM_NODES)
        x = jax.nn.relu(x)
        x = gcn_conv(x, W2, b2, src, dst, NUM_NODES)
        return x

    def _L0_ffn_ref(x, Wr, br, W1, b1, W2, b2, gamma, beta):
        import math
        import jax, jax.numpy as jnp
        import numpy as np
        CAPACITY_FACTOR = 1.25
        TOP_K = 2
        LN_EPS = 1e-05

        def _layer_norm(x, gamma, beta):
            mu = jnp.mean(x, axis=-1, keepdims=True)
            var = jnp.var(x, axis=-1, keepdims=True)
            return (x - mu) * jax.lax.rsqrt(var + LN_EPS) * gamma + beta
        B, S, D = x.shape
        E = Wr.shape[1]
        N = B * S
        K = TOP_K
        logits = jnp.mean(x, axis=1) @ Wr + br
        routing_weights = jax.nn.softmax(logits, axis=-1)
        capacity = float(math.ceil(N * CAPACITY_FACTOR / E))
        expected_loads = routing_weights.sum(axis=0) * (N / B)
        scale = jnp.where(expected_loads > capacity, capacity / expected_loads, 1.0)
        routing_weights = jax.nn.softmax(routing_weights * scale, axis=-1)
        rw_tok = jnp.broadcast_to(routing_weights[:, None, :], (B, S, E)).reshape(N, E)
        top_w, top_i = jax.lax.top_k(rw_tok, K)
        top_w = jax.nn.softmax(top_w, axis=-1)
        xf = x.reshape(N, D)
        h = jax.nn.gelu(jnp.einsum('nd,edf->enf', xf, W1) + b1[:, None, :], approximate=False)
        y = jnp.einsum('enf,efd->end', h, W2) + b2[:, None, :]
        w_dense = jnp.zeros((N, E), x.dtype).at[jnp.arange(N)[:, None], top_i].add(top_w)
        out = jnp.einsum('ne,end->nd', w_dense, y).reshape(B, S, D)
        out = _layer_norm(out + x, gamma, beta)
        return out

    def _L1_gnn_ref(x, edge_index, W, att_src, att_dst, bias):
        import jax, jax.numpy as jnp
        import numpy as np
        N_NODES = 50000
        N_EDGES = 25000
        IN_FEAT = 256
        HEADS = 4
        OUT_FEAT = 64
        NEG_SLOPE = 0.2
        N = x.shape[0]
        H, C = att_src.shape
        h = (x @ W).reshape(N, H, C)
        a_src = jnp.sum(h * att_src[None], axis=-1)
        a_dst = jnp.sum(h * att_dst[None], axis=-1)
        loop = jnp.arange(N, dtype=edge_index.dtype)
        src = jnp.concatenate([edge_index[0], loop])
        dst = jnp.concatenate([edge_index[1], loop])
        alpha = jax.nn.leaky_relu(a_src[src] + a_dst[dst], NEG_SLOPE)
        m = jax.ops.segment_max(alpha, dst, num_segments=N)
        alpha = jnp.exp(alpha - jax.lax.stop_gradient(m)[dst])
        denom = jax.ops.segment_sum(alpha, dst, num_segments=N)
        alpha = alpha / (denom[dst] + 1e-16)
        msg = h[src] * alpha[:, :, None]
        out = jax.ops.segment_sum(msg, dst, num_segments=N)
        out = out.reshape(N, H * C) + bias
        return jax.nn.relu(out)

    def _L1_ffn_ref(x, gate_w, gate_b, W1, b1, W2, b2):
        import jax, jax.numpy as jnp
        import numpy as np
        B, T, D, H, E = (16, 128, 256, 512, 8)
        Bb, Tt, Dd = x.shape
        Ee = gate_w.shape[1]
        xf = x.reshape(-1, Dd)
        N = xf.shape[0]
        logits = xf @ gate_w + gate_b
        probs = jax.nn.softmax(logits, axis=-1)
        top2_vals, top2_idx = jax.lax.top_k(probs, 2)
        cw = jnp.zeros((N, Ee), dtype=xf.dtype).at[jnp.arange(N)[:, None], top2_idx].add(top2_vals)

        def step(acc, params):
            w1, bb1, w2, bb2, we = params
            h = jax.nn.gelu(xf @ w1 + bb1, approximate=False)
            y = h @ w2 + bb2
            return (acc + we[:, None] * y, None)
        out, _ = jax.lax.scan(step, jnp.zeros_like(xf), (W1, b1, W2, b2, cw.T))
        return out.reshape(Bb, Tt, Dd)
    edge_index = jnp.stack([src, dst])
    x = x + _L0_gnn_ref(_layernorm(x, axis=-1), L0_gnn_W1, L0_gnn_b1, L0_gnn_W2, L0_gnn_b2, edge_index)
    x = x + _L0_ffn_ref(_layernorm(x, axis=-1)[None], L0_ffn_Wr, L0_ffn_br, L0_ffn_W1, L0_ffn_b1, L0_ffn_W2, L0_ffn_b2, L0_ffn_gamma, L0_ffn_beta)[0]
    x = x + _L1_gnn_ref(_layernorm(x, axis=-1), edge_index, L1_gnn_W, L1_gnn_att_src, L1_gnn_att_dst, L1_gnn_bias)
    x = x + _L1_ffn_ref(_layernorm(x, axis=-1)[None], L1_ffn_gate_w, L1_ffn_gate_b, L1_ffn_W1, L1_ffn_b1, L1_ffn_W2, L1_ffn_b2)[0]
    return x

_drawn_inputs = setup_inputs


def setup_inputs(seed=0):
    import zlib

    import numpy as np

    out = dict(_drawn_inputs(seed))
    spreads = {'L0_gnn_b1': (0.0, 0.1),
     'L0_gnn_b2': (0.0, 0.1),
     'L0_ffn_br': (0.0, 0.1),
     'L0_ffn_b1': (0.0, 0.36),
     'L0_ffn_b2': (0.0, 0.1),
     'L0_ffn_gamma': (1.0, 0.2),
     'L0_ffn_beta': (0.0, 0.1),
     'L1_ffn_gate_b': (0.0, 0.8),
     'L1_ffn_b1': (0.0, 0.8),
     'L1_ffn_b2': (0.0, 0.631)}
    factors = {'L1_gnn_att_dst': 5.226,
     'L1_gnn_bias': 8.0,
     'L1_ffn_gate_w': 3.983,
     'L1_ffn_W1': 5.769,
     'L1_ffn_W2': 5.372}
    for name, (base, spread) in spreads.items():
        noise = np.random.default_rng([zlib.crc32(name.encode()), seed]).standard_normal(out[name].shape)
        drawn = base * np.exp(spread * noise) if base else spread * noise
        out[name] = jnp.asarray(drawn.astype(out[name].dtype))
    for name, factor in factors.items():
        out[name] = (out[name] * factor).astype(out[name].dtype)
    return out
```

```python
from contextlib import ExitStack

import concourse.bass as bass
from concourse import mybir

ALU = mybir.AluOpType
ACT = mybir.ActivationFunctionType
AX = mybir.AxisListType
F32 = mybir.dt.float32
BF16 = mybir.dt.bfloat16
I32 = mybir.dt.int32

P = 128
N, D = 3125, 256
E = 50000
HID = 128
NB = -(-N // P)
TAIL = N - (NB - 1) * P
NPAD = NB * P
GB = 5
NG = NB // GB
ET = -(-E // P)
EC = -(-ET // P)
HALF = 8
PARTS, PS = 4, 4
STEPS = -(-(ET + NB - 1) // (2 * HALF)) * 2 * HALF
IT = STEPS // (2 * HALF)
LOOK = 18
EPS = 1e-5
NE = 8
FF = 512
FC = FF // P
CH = [4] * (NB // 4) + [NB % 4]
C0 = [4 * c for c in range(len(CH))]
UN = 2 * len(CH)
HEADS = 4
HC = D // HEADS
ROW = D + 2 * HEADS
KC = STEPS // 4
BIG = 1e38
SLOPE = 0.2
CAP = float(-(-N * 5 // (4 * NE)))
assert NB == NG * GB


class Chain:

    def __init__(self, eng, sem):
        self.eng, self.sem, self.n, self.i, self.per = eng, sem, 0, None, 0

    def value(self):
        return self.n if self.i is None else self.i * self.per + self.n

    def mark(self, ins):
        self.n += 1
        return ins.then_inc(self.sem, 1)

    def link(self, ins):
        self.mark(ins)
        self.eng.wait_ge(self.sem, self.value())

    def enter(self, i, per):
        self.i, self.per, self.first = i, per, self.n

    def leave(self, times):
        assert self.n - self.first == self.per, (self.n - self.first, self.per)
        self.i = None
        self.n = self.first + times * self.per


def build(nc, a, out):
    with ExitStack() as ctx:
        def sb(name, shape, dt=F32):
            return ctx.enter_context(nc.sbuf_tensor(name, shape, dt))

        def sem(name):
            return ctx.enter_context(nc.semaphore(name))

        table1 = nc.dram_tensor("table1", (NPAD, HID), F32).ap()
        table2 = nc.dram_tensor("table2", (NPAD, HID), F32).ap()
        table3 = nc.dram_tensor("table3", (NPAD, D), F32).ap()
        table_a = nc.dram_tensor("table_a", (NPAD, 2 * HEADS), F32).ap()
        src_low = nc.dram_tensor("src_low", (STEPS, P), BF16).ap()
        dst_low = nc.dram_tensor("dst_low", (STEPS, P), BF16).ap()

        X = sb("X", [P, NB, D])
        XTF = sb("XTF", [P, NB * ROW])
        XT = XTF[:, 0:2 * NPAD].rearrange("p (k n) -> p k n", k=2)
        ACC = XTF[:, :].rearrange("p (b n) -> p b n", b=NB)
        H = sb("H", [P, NB, D])
        XN = sb("XN", [P, NB, D])
        stats = sb("stats", [P, NB, 6])
        mv = sb("mv", [P, NB, 2])
        rstd = sb("rstd", [P, NB])
        eps = sb("eps", [P, 1])
        one = sb("one", [P, 1])
        iotaK = sb("iotaK", [P, STEPS])
        iotaP = sb("iotaP", [P, 1])
        ident = sb("ident", [P, P])
        zeros = sb("zeros", [P, 512], BF16)
        shared = sb("shared", [P, 8192])
        taken = [0]

        def view(shape, dt=F32, start=None):
            if start is not None:
                taken[0] = start
            size = 1
            for n in shape[1:]:
                size *= n
            words = size // 2 if dt == BF16 else size
            ap = shared[0:shape[0], taken[0]:taken[0] + words]
            taken[0] += words
            assert taken[0] <= 8192
            if dt != F32:
                ap = ap.bitcast(dt)
            names = ["a", "b", "c", "d"][:len(shape) - 1]
            return ap if len(names) == 1 else ap.rearrange("p (" + " ".join(names) + ") -> p " + " ".join(names), **dict(zip(names, shape[1:])))

        SI = view([P, EC, P], I32, start=0)
        DI = view([P, EC, P], I32)
        SF = view([P, EC, P])
        DF = view([P, EC, P])
        S = view([P, EC, STEPS])
        HSEL = view([P, 2, HALF, NB], BF16)
        OHB = view([P, 2, HALF, P], BF16)
        DR = view([KC, 4, P])
        SRI = view([KC, 4, P], I32)
        LFR = view([KC, 4, P])
        lowS = view([KC, 4, P], BF16)
        lowD = view([KC, 4, P], BF16)
        BRS = view([P, 2, HALF * P], BF16, start=0)
        BRD = view([P, 2, HALF * P], BF16)
        OTS = view([P, 2, HALF * P], BF16)
        OTD = view([P, 2, HALF * P], BF16)
        MSK = view([P, 2, HALF * NB])
        SELV = view([P, 2, HALF * NB, HEADS])
        WA = view([P, 2, D])
        attbc = view([P, 2, D])
        SCF = view([KC, 4, HEADS, P], start=0)
        SCB = view([KC, 4, HEADS, P])
        PG = view([P, STEPS, 2 * HEADS])
        W1E = view([P, 2, 2, FF], start=0)
        W2E = view([P, 2, FC, D])
        HT = view([P, 2, FC, FF])
        xnf = XN[:, :, :].rearrange("p b n -> p (b n)")
        V = xnf[:, 0:STEPS * HEADS].rearrange("p (k h) -> p k h", h=HEADS)
        AD = xnf[:, STEPS * HEADS:STEPS * HEADS * 3].rearrange("p (k h) -> p k h", h=2 * HEADS)
        EPI = sb("EPI", [P, EC], I32)
        ELI = sb("ELI", [P, EC], I32)
        tcol = sb("tcol", [P, EC])
        tlo = sb("tlo", [P, EC])
        thi = sb("thi", [P, EC])
        IDX = sb("IDX", [P, STEPS], I32)
        DLOC = sb("DLOC", [P, STEPS])
        BLKI2 = sb("BLKI2", [P, STEPS], I32)
        BLKF = sb("BLKF", [P, STEPS])
        BLKI = sb("BLKI", [P, STEPS], I32)
        OH = sb("OH", [P, 2, HALF, P])
        IDXS = sb("IDXS", [P, 2, HALF, 1], I32)
        ring = sb("ring", [P, 2, HALF, ROW])
        RING4, OH4, IDXS4 = (t[:, :, :, :].rearrange("p h (g s) n -> p (h g) s n", s=PS) for t in (ring, OH, IDXS))
        dinv = sb("dinv", [P, NB])
        W1 = sb("W1", [P, 2, HID])
        W2 = sb("W2", [P, D])
        b1bc = sb("b1bc", [P, HID])
        b2bc = sb("b2bc", [P, D])

        stage = sb("stage", [P, 2, HALF, 2 * HEADS])
        SHI = sb("SHI", [P, STEPS])
        LFT = sb("LFT", [P, STEPS])
        NFX = sb("NFX", [KC, 4, P + 1])
        krow = sb("krow", [KC, 4])
        bcol = sb("bcol", [KC, 4])
        lf127 = sb("lf127", [KC, 4, HEADS])
        brkF = sb("brkF", [HEADS, STEPS])
        brkB = sb("brkB", [HEADS, STEPS])
        newF = sb("newF", [HEADS, STEPS])
        lev = sb("lev", [HEADS, 2, STEPS])
        car = sb("car", [HEADS, 2, STEPS])
        cin = sb("cin", [KC, 2, 4, HEADS])
        ends = sb("ends", [KC, 2, 4, HEADS])
        WG = sb("WG", [P, 2, ROW])
        A8 = sb("A8", [P, NB, 2 * HEADS])
        A8R = sb("A8R", [P, NB, 2 * HEADS])
        A8P = sb("A8P", [P, NB, 3, 2 * HEADS], BF16)
        node = sb("node", [P, 5, NB, HEADS])
        biasbc = sb("biasbc", [P, D])
        biasT = sb("biasT", [P, NE * FC])
        biasS = sb("biasS", [P, 2 * FC])
        msum = sb("msum", [P, 2, NG])
        mean = sb("mean", [P, 2])
        Wr = sb("Wr", [P, 2, NE])
        brbc = sb("brbc", [P, NE])
        b1rows = sb("b1rows", [NE, FF])
        b2rows = sb("b2rows", [NE, D])
        rt = sb("rt", [P, 8, NE])
        rs = sb("rs", [P, 16])
        topi = sb("topi", [P, NE], mybir.dt.uint32)
        topf = sb("topf", [P, NE])
        sel = sb("sel", [NE, 3])
        gate = sb("gate", [P, 2, NE])
        gbbc = sb("gbbc", [P, NE])
        b1r32 = sb("b1r32", [NE * FC, P])
        b2rows2 = sb("b2rows2", [NE, D])
        LOW = sb("LOW", [P, NE, NE])
        CW = sb("CW", [P, NB, NE])
        hf = H[:, :, :].rearrange("p b n -> p (b n)")
        GT = hf[:, 0:NB * NE * NE].rearrange("p (b e j) -> p b e j", e=NE, j=NE)
        EQ = hf[:, NB * NE * NE:2 * NB * NE * NE].rearrange("p (b e j) -> p b e j", e=NE, j=NE)
        RK = hf[:, NB * D - NB * NE:NB * D].rearrange("p (b e) -> p b e", e=NE)
        CWT = hf[0:NE, NB * NE * NE:NB * NE * NE + NPAD]
        gambc = sb("gambc", [P, D])
        betbc = sb("betbc", [P, D])

        ps = ctx.enter_context(nc.psum_tensor("ps", [P, 8, 512], F32))
        flat = ps[:, :, :].rearrange("p b n -> p (b n)")
        acc = flat[:, 0:NB * HID]

        x_in = [sem(f"x_in{g}") for g in range(NG)]
        w_in = sem("w_in")
        pads = sem("pads")
        edges_in = sem("edges_in")
        consts = sem("consts")
        dve_op = sem("dve_op")
        ln_ready = sem("ln_ready")
        tr_ready = sem("tr_ready")
        xt_ready = sem("xt_ready")
        sel_ready = sem("sel_ready")
        steps_ps = sem("steps_ps")
        steps_ready = sem("steps_ready")
        ohb_ready = [sem(f"ohb_ready{h}") for h in range(2)]
        ohb_used = [sem(f"ohb_used{h}") for h in range(2)]
        zeroed = sem("zeroed")
        h1_ps = sem("h1_ps")
        h1_ready = sem("h1_ready")
        t_out = sem("t_out")
        idx_ready = [sem(f"idx_ready{h}") for h in range(2)]
        gathered = [sem(f"gathered{h}") for h in range(2)]
        oh_ready = [sem(f"oh_ready{h}") for h in range(2)]
        step_used = [sem(f"step_used{h}") for h in range(2)]
        agg_done = sem("agg_done")
        agg_free = sem("agg_free")
        z_ready = sem("z_ready")
        aggT_ps = sem("aggT_ps")
        aggT_ready = sem("aggT_ready")
        o_ps = sem("o_ps")
        x_ready = sem("x_ready")
        final = sem("final")
        pair_begun = sem("pair_begun")
        pair_bias = sem("pair_bias")
        low1 = sem("low1")
        gate_in = sem("gate_in")
        gate_ps = sem("gate_ps")
        gmax_ready = sem("gmax_ready")
        gexp_ready = sem("gexp_ready")
        cw_ready = sem("cw_ready")
        cwt_ps = sem("cwt_ps")
        cwt_ready = sem("cwt_ready")
        b1t_ps = sem("b1t_ps")
        b1t_ready = sem("b1t_ready")
        b2_ps = sem("b2_ps")
        b2_taken = sem("b2_taken")
        rows_ps = sem("rows_ps")
        low_ready = sem("low_ready")
        low_out = sem("low_out")
        ends_ps = sem("ends_ps")
        dr_ready = sem("dr_ready")
        f0_ready = sem("f0_ready")
        lf_ps = sem("lf_ps")
        lfr_ready = sem("lfr_ready")
        lft_ps = sem("lft_ps")
        prep_done = sem("prep_done")
        att_in = sem("att_in")
        wg_ready = sem("wg_ready")
        h3_ps = sem("h3_ps")
        h3_ready = sem("h3_ready")
        split_ready = sem("split_ready")
        br_in = [sem(f"br_in{h}") for h in range(2)]
        ot_ready = [sem(f"ot_ready{h}") for h in range(2)]
        look_ps = [sem(f"look_ps{h}") for h in range(2)]
        v_taken = [sem(f"v_taken{h}") for h in range(2)]
        ad_taken = [sem(f"ad_taken{h}") for h in range(2)]
        v_ready = sem("v_ready")
        a_out = sem("a_out")
        va_idx = [sem(f"va_idx{h}") for h in range(2)]
        va_in = [sem(f"va_in{h}") for h in range(2)]
        va_out = [sem(f"va_out{h}") for h in range(2)]
        va_turn = sem("va_turn")
        msk_ready = [sem(f"msk_ready{h}") for h in range(2)]
        vrow_ps = sem("vrow_ps")
        ends_ready = sem("ends_ready")
        lev_ps = sem("lev_ps")
        car_ready = sem("car_ready")
        cin_ps = sem("cin_ps")
        max_ready = sem("max_ready")
        max_ps = sem("max_ps")
        gap_ready = sem("gap_ready")
        pg_ready = sem("pg_ready")
        slot_idx = [sem(f"slot_idx{q}") for q in range(PARTS)]
        slot_in = [sem(f"slot_in{q}") for q in range(PARTS)]
        slot_oh = [sem(f"slot_oh{q}") for q in range(PARTS)]
        slot_msg = [sem(f"slot_msg{q}") for q in range(PARTS)]
        slot_used = [sem(f"slot_used{q}") for q in range(PARTS)]
        quad_taken = sem("quad_taken")
        self_in = sem("self_in")
        self_out = sem("self_out")
        moe_in = sem("moe_in")
        mean_ready = sem("mean_ready")
        logits_ps = sem("logits_ps")
        exp_in = sem("exp_in")
        exp_out = sem("exp_out")
        sel_out = sem("sel_out")
        route_done = sem("route_done")
        bias_ps = sem("bias_ps")
        bias_ready = sem("bias_ready")
        w_ready = [sem(f"w_ready{k}") for k in range(2)]
        h_ps = sem("h_ps")
        h_ready = sem("h_ready")
        y_ps = sem("y_ps")
        y_taken = sem("y_taken")
        target_ready = sem("target_ready")
        deg_ps = sem("deg_ps")
        gathers_begun = sem("gathers_begun")
        var_ready = sem("var_ready")
        std_ready = sem("std_ready")
        deg_root = sem("deg_root")

        block = ctx.enter_context(nc.Block())

        @block.sync
        def _(sp):
            sp.wait_ge(pads, 5)
            full = ET // P * P * P
            for dst_sb, src_d in ((SI, a["src"]), (DI, a["dst"])):
                sp.dma_start(dst_sb[:, 0:ET // P, :], src_d[0:full].rearrange("(c p e) -> p c e", p=P, e=P)).then_inc(edges_in, 16)
                more = (E - full) // P
                sp.dma_start(dst_sb[0:more, EC - 1, :], src_d[full:full + more * P].rearrange("(p e) -> p e", e=P)).then_inc(edges_in, 16)
                rest = E - full - more * P
                sp.dma_start(dst_sb[more:more + 1, EC - 1, 0:rest], src_d[E - rest:E].rearrange("(p e) -> p e", p=1)).then_inc(edges_in, 16)
            last = a["dst"][0:(ET - 1) * P].rearrange("(t e) -> t e", e=P)[:, P - 1:P]
            sp.dma_start(EPI[1:P, 0:1], last[0:P - 1, :], allow_slow_non_contiguous=True).then_inc(edges_in, 16)
            for c in range(1, EC):
                n = min(P, ET - c * P)
                sp.dma_start(EPI[0:n, c:c + 1], last[c * P - 1:c * P - 1 + n, :], allow_slow_non_contiguous=True).then_inc(edges_in, 16)
            for g in range(NG):
                if g < NG - 1:
                    sp.dma_start(X[:, g * GB:(g + 1) * GB, :], a["x"][g * GB * P:(g + 1) * GB * P, :].rearrange("(b p) d -> p b d", p=P)).then_inc(x_in[g], 16)
                else:
                    sp.dma_start(X[:, g * GB:NB - 1, :], a["x"][g * GB * P:(NB - 1) * P, :].rearrange("(b p) d -> p b d", p=P)).then_inc(x_in[g], 16)
                    sp.dma_start(X[0:TAIL, NB - 1, :], a["x"][(NB - 1) * P:N, :]).then_inc(x_in[g], 16)
            sp.dma_start(W1[:, :, :], a["L0_gnn_W1"].rearrange("(k p) n -> p k n", p=P)).then_inc(w_in, 16)
            sp.dma_start(W2[:, :], a["L0_gnn_W2"]).then_inc(w_in, 16)
            sp.dma_start(b1bc[:, :], a["L0_gnn_b1"].partition_broadcast(P)).then_inc(w_in, 16)
            sp.dma_start(b2bc[:, :], a["L0_gnn_b2"].partition_broadcast(P)).then_inc(w_in, 16)
            sp.wait_ge(low_ready, 2)
            sp.dma_start(src_low.rearrange("(c p) e -> p c e", p=KC), lowS[:, :, :]).then_inc(low_out, 16)
            sp.dma_start(dst_low.rearrange("(c p) e -> p c e", p=KC), lowD[:, :, :]).then_inc(low_out, 16)
            for n, table in enumerate((table1, table2)):
                tg = table.rearrange("(g b p) n -> g p b n", b=GB, p=P)
                for g in range(NG):
                    sp.wait_ge(h1_ready, n * NG + g + 1)
                    sp.dma_start(tg[g], H[:, g * GB:(g + 1) * GB, 0:HID]).then_inc(t_out, 16)
            ff0 = {k: a["L0_ffn_" + k] for k in ("Wr", "br", "W1", "b1", "W2", "b2", "gamma", "beta")}
            sp.dma_start(Wr[:, :, :], ff0["Wr"].rearrange("(k p) e -> p k e", p=P)).then_inc(moe_in, 16)
            sp.dma_start(brbc[:, :], ff0["br"].partition_broadcast(P)).then_inc(moe_in, 16)
            sp.dma_start(b1rows[:, :], ff0["b1"]).then_inc(moe_in, 16)
            sp.dma_start(b2rows[:, :], ff0["b2"]).then_inc(moe_in, 16)
            sp.dma_start(gambc[:, :], ff0["gamma"].partition_broadcast(P)).then_inc(moe_in, 16)
            sp.dma_start(betbc[:, :], ff0["beta"].partition_broadcast(P)).then_inc(moe_in, 16)
            sp.wait_ge(route_done, 1)
            taken = [sp.alloc_register(f"taken{k}") for k in range(2)]
            sp.load(taken, topi[0:1, 0:2])
            for k in range(2):
                e = sp.snap(taken[k], min_val=0, max_val=NE - 1)
                sp.dma_start(W1E[:, k, :, :], ff0["W1"].rearrange("e (k p) f -> p e k f", p=P)[:, bass.ds(e, 1), :, :]).then_inc(w_ready[k], 16)
                sp.dma_start(W2E[:, k, :, :], ff0["W2"].rearrange("e (c p) d -> p e c d", p=P)[:, bass.ds(e, 1), :, :]).then_inc(w_ready[k], 16)
            sp.dma_start(WG[:, :, 0:D], a["L1_gnn_W"].rearrange("(k p) n -> p k n", p=P)).then_inc(att_in, 16)
            sp.dma_start(biasbc[:, :], a["L1_gnn_bias"].partition_broadcast(P)).then_inc(att_in, 16)
            sp.wait_ge(y_ps, UN + 2)
            sp.dma_start(attbc[:, 0, :], a["L1_gnn_att_src"].rearrange("h c -> (h c)").partition_broadcast(P)).then_inc(att_in, 16)
            sp.dma_start(attbc[:, 1, :], a["L1_gnn_att_dst"].rearrange("h c -> (h c)").partition_broadcast(P)).then_inc(att_in, 16)
            for c in range(len(CH)):
                sp.wait_ge(h3_ready, 2 * c + 2)
                sp.dma_start(table3[C0[c] * P:(C0[c] + CH[c]) * P, :].rearrange("(b p) n -> p b n", p=P), H[:, C0[c]:C0[c] + CH[c], :]).then_inc(t_out, 16)
            sp.dma_start(table_a.rearrange("(b p) n -> p b n", p=P), A8[:, :, :]).then_inc(a_out, 16)
            sp.wait_ge(low_out, 32)
            with sp.Fori(0, LOOK) as i:
                for h in range(2):
                    sp.wait_ge(ot_ready[h], i * 2 + 1)
                    at = (i * 2 + h) * (HALF * P)
                    sp.dma_start(BRS[:, h, :], src_low.rearrange("k e -> (k e)")[bass.ds(at, HALF * P)].partition_broadcast(P)).then_inc(br_in[h], 16)
                    sp.dma_start(BRD[:, h, :], dst_low.rearrange("k e -> (k e)")[bass.ds(at, HALF * P)].partition_broadcast(P)).then_inc(br_in[h], 16)
            with sp.Fori(LOOK, IT) as i:
                for h in range(2):
                    sp.wait_ge(ot_ready[h], i * 2 + 1)
                    sp.dma_start(BRD[:, h, :], dst_low.rearrange("k e -> (k e)")[bass.ds((i * 2 + h) * (HALF * P), HALF * P)].partition_broadcast(P)).then_inc(br_in[h], 16)
            ff1 = {k: a["L1_ffn_" + k] for k in ("gate_w", "gate_b", "W1", "b1", "W2", "b2")}
            sp.dma_start(gate[:, :, :], ff1["gate_w"].rearrange("(k p) e -> p k e", p=P)).then_inc(gate_in, 16)
            sp.dma_start(gbbc[:, :], ff1["gate_b"].partition_broadcast(P)).then_inc(gate_in, 16)
            sp.dma_start(b1r32[:, :], ff1["b1"].rearrange("e (c p) -> (e c) p", p=P)).then_inc(gate_in, 16)
            sp.dma_start(b2rows2[:, :], ff1["b2"]).then_inc(gate_in, 16)
            sp.wait_ge(self_in, 1)
            with sp.Fori(0, NE // 2) as i:
                for k in range(2):
                    sp.wait_ge(y_ps, i * UN + (len(CH) * (k + 1) + 2))
                    sp.dma_start(W1E[:, k, :, :], ff1["W1"].rearrange("e (k p) f -> p e k f", p=P)[:, bass.ds(i * 2 + k, 1), :, :]).then_inc(w_ready[k], 16)
                    sp.dma_start(W2E[:, k, :, :], ff1["W2"].rearrange("e (c p) d -> p e c d", p=P)[:, bass.ds(i * 2 + k, 1), :, :]).then_inc(w_ready[k], 16)
            for c in range(len(CH)):
                sp.wait_ge(y_taken, (NE // 2 + 1) * UN + 3 + c - len(CH))
                if c < len(CH) - 1:
                    sp.dma_start(out[C0[c] * P:(C0[c] + CH[c]) * P, :].rearrange("(b p) d -> p b d", p=P), X[:, C0[c]:C0[c] + CH[c], :]).then_inc(final, 16)
                else:
                    sp.dma_start(out[C0[c] * P:N, :], X[0:TAIL, C0[c], :]).then_inc(final, 16)
            sp.wait_ge(final, 16 * len(CH))

        @block.gpsimd
        def _(pool):
            pool.memset(SI[:, :, :], 0).then_inc(pads, 1)
            pool.memset(DI[:, :, :], NPAD - 1).then_inc(pads, 1)
            pool.memset(EPI[:, :], NPAD - 1).then_inc(pads, 1)
            pool.wait_ge(pads, 3)
            pool.memset(EPI[0:1, 0:1], 0).then_inc(pads, 1)
            pool.memset(X[:, NB - 1, :], 0.0).then_inc(pads, 1)
            pool.iota(iotaK[:, :], [[1, STEPS]], base=0, channel_multiplier=0, allow_small_or_imprecise_dtypes=True).then_inc(consts, 1)
            pool.iota(iotaP[:, :], [[0, 1]], base=0, channel_multiplier=1, allow_small_or_imprecise_dtypes=True).then_inc(consts, 1)
            pool.iota(tcol[:, :], [[P, EC]], base=0, channel_multiplier=1, allow_small_or_imprecise_dtypes=True).then_inc(consts, 1)
            pool.iota(krow[:, :], [[KC, 4]], base=0, channel_multiplier=1, allow_small_or_imprecise_dtypes=True).then_inc(consts, 1)
            pool.memset(NFX[:, :, :], 0.0).then_inc(consts, 1)
            pool.memset(LOW[:, :, :], 1.0).then_inc(low1, 1)
            pool.wait_ge(low1, 1)
            pool.affine_select(out=LOW[:, :, :], in_=LOW[:, :, :], compare_op=ALU.is_gt, fill=0.0, base=0,
                               pattern=[[1, NE], [-1, NE]], channel_multiplier=0).then_inc(low1, 1)
            pool.memset(zeros[:, :], 0.0).then_inc(consts, 1)
            pool.memset(ident[:, :], 0.0).then_inc(consts, 1)
            pool.memset(eps[:, :], EPS).then_inc(consts, 1)
            pool.memset(one[:, :], 1.0).then_inc(consts, 1)
            pool.wait_ge(consts, 9)
            pool.affine_select(out=ident[:, :], in_=ident[:, :], compare_op=ALU.not_equal, fill=1.0, base=0,
                               pattern=[[-1, P]], channel_multiplier=1).then_inc(consts, 1)

            def gather_pass(n, table, width, written):
                pool.wait_ge(t_out, 16 * written)
                with pool.Fori(0, IT) as i:
                    for h in range(2):
                        pool.wait_ge(idx_ready[h], i + (n * IT + 1))
                        pool.sem_inc(gathers_begun, 1)
                        for s in range(HALF):
                            pool.indirect_dma_start(ring[:, h, s, 0:width], None, table[:, :],
                                                    bass.IndirectOffsetOnAxis(ap=IDXS[:, h, s, :], axis=0)).then_inc(gathered[h], 16)

            gather_pass(0, table1, HID, NG)
            gather_pass(1, table2, HID, 2 * NG)
            pool.wait_ge(a_out, 16)
            with pool.Fori(0, IT - LOOK) as i:
                for h in range(2):
                    pool.wait_ge(va_idx[h], i + 1)
                    pool.sem_inc(gathers_begun, 1)
                    for s in range(HALF):
                        pool.indirect_dma_start(stage[:, h, s, :], None, table_a[:, :],
                                                bass.IndirectOffsetOnAxis(ap=IDXS[:, h, s, :], axis=0)).then_inc(va_in[h], 16)
            pool.wait_ge(t_out, 16 * (2 * NG + len(CH)))
            with pool.Fori(0, IT) as i:
                for q in range(PARTS):
                    pool.wait_ge(slot_idx[q], i + 1)
                    pool.sem_inc(gathers_begun, 1)
                    for s in range(PS):
                        pool.indirect_dma_start(RING4[:, q, s, 0:D], None, table3[:, :],
                                                bass.IndirectOffsetOnAxis(ap=IDXS4[:, q, s, :], axis=0)).then_inc(slot_in[q], 16)

        @block.scalar
        def _(act):
            def transpose_out(n, sums=False, count=None):
                count = count or n + 1
                act.wait_ge(var_ready, count)
                act.activation(rstd[:, :], mv[:, :, 1], ACT.Sqrt, bias=eps[:, 0:1]).then_inc(std_ready, 1)
                for g in range(NG):
                    act.wait_ge(tr_ready, n * NG + g + 1)
                    for k in range(2):
                        ins = act.activation(XT[:, k, g * GB * P:(g + 1) * GB * P], flat[:, k * GB * P:(k + 1) * GB * P], ACT.Copy,
                                             **(dict(accum_out=msum[:, k, g:g + 1]) if sums else {}))
                        ins.then_inc(xt_ready, 1)

            def index_slots(n):
                with act.Fori(0, IT) as i:
                    for h in range(2):
                        act.wait_ge(step_used[h], i + (n * IT + 1))
                        act.activation(IDXS[:, h, :, 0], IDX[:, bass.ds(i * (2 * HALF) + h * HALF, HALF)], ACT.Copy).then_inc(idx_ready[h], 1)

            act.wait_ge(consts, 10)
            transpose_out(0)
            act.wait_ge(steps_ready, 1)
            act.wait_ge(deg_ps, 1)
            act.activation(dinv[:, :], ps[:, 3, 0:NB], ACT.Sqrt, bias=one[:, 0:1]).then_inc(deg_root, 1)
            index_slots(0)
            index_slots(1)
            for g in range(NG):
                act.wait_ge(aggT_ps, g + 1)
                act.activation(XT[:, 0, g * GB * P:(g + 1) * GB * P], flat[:, 0:GB * P], ACT.Copy).then_inc(aggT_ready, 1)
            transpose_out(1, sums=True)
            for n in range(3):
                act.wait_ge(exp_in, n + 1)
                w = 2 if n == 2 else NE
                act.activation(rt[:, 2 * n + 1, 0:w], rt[:, 2 * n, 0:w], ACT.Exp, bias=rs[:, n:n + 1], accum_out=rs[:, 4 + n:5 + n]).then_inc(exp_out, 1)

            def gelus(base, i, biases):
                for u in range(UN):
                    U = (0 if i is None else i * UN) + base + u
                    k, c = divmod(u, len(CH))
                    act.wait_ge(y_ps, U + 1)
                    n = CH[c] * P
                    for f in range(FC):
                        act.wait_ge(h_ps, U * FC + (f + 1))
                        b = k * FC + f
                        act.activation(HT[:, u % 2, f, 0:n], ps[:, f, 0:n], ACT.Gelu, bias=biases[:, b:b + 1]).then_inc(h_ready, 1)

            act.wait_ge(bias_ready, 1)
            gelus(0, None, biasT)
            act.wait_ge(var_ready, 3)
            act.activation(rstd[:, :], mv[:, :, 1], ACT.Sqrt, bias=eps[:, 0:1]).then_inc(std_ready, 1)
            transpose_out(2, count=4)
            for c in range(len(CH)):
                act.wait_ge(h3_ps, c + 1)
                q = 4 * (c % 2)
                act.activation(A8[:, C0[c]:C0[c] + CH[c], :], ps[:, q:q + CH[c], D:ROW], ACT.Copy).then_inc(h3_ready, 1)
                act.activation(H[:, C0[c]:C0[c] + CH[c], :], ps[:, q:q + CH[c], 0:D], ACT.Copy).then_inc(h3_ready, 1)
            def va_index(i, h):
                act.activation(IDXS[:, h, :, 0], IDX[:, bass.ds(i * (2 * HALF) + (2 * LOOK + h) * HALF, HALF)], ACT.Copy).then_inc(va_idx[h], 1)

            def va_copy(i, h):
                act.wait_ge(va_in[h], i * (16 * HALF) + 16 * HALF)
                act.sem_inc(va_turn, 1)
                act.activation(V[:, bass.ds(i * (2 * HALF) + (2 * LOOK + h) * HALF, HALF), :], stage[:, h, :, 0:HEADS], ACT.Copy).then_inc(va_out[h], 1)

            va_index(0, 0)
            va_index(0, 1)
            with act.Fori(0, IT - LOOK - 1) as i:
                for h in range(2):
                    va_copy(i, h)
                    va_index(i + 1, h)
            for h in range(2):
                va_copy(IT - LOOK - 1, h)
            act.wait_ge(gap_ready, 1)
            act.activation(PG[:, :, 0:HEADS], V[:, :, :], ACT.Exp).then_inc(pg_ready, 1)
            with act.Fori(0, IT) as i:
                for q in range(PARTS):
                    act.wait_ge(slot_used[q], i + 1)
                    act.activation(IDXS4[:, q, :, 0], IDX[:, bass.ds(i * (PARTS * PS) + q * PS, PS)], ACT.Copy).then_inc(slot_idx[q], 1)
            act.wait_ge(self_in, 1)
            act.activation(node[:, 3, :, :], node[:, 2, :, :], ACT.Exp).then_inc(self_out, 1)
            transpose_out(3, count=5)
            act.wait_ge(gmax_ready, 1)
            act.activation(CW[:, :, :], CW[:, :, :], ACT.Exp).then_inc(gexp_ready, 1)
            act.wait_ge(b1t_ps, 1)
            act.activation(biasT[:, :], ps[:, 7, 0:NE * FC], ACT.Copy).then_inc(b1t_ready, 1)
            for c in range(len(CH)):
                act.wait_ge(cwt_ps, c + 1)
                act.activation(CWT[:, C0[c] * P:(C0[c] + CH[c]) * P], ps[0:NE, c, 0:CH[c] * P], ACT.Copy).then_inc(cwt_ready, 1)
            act.wait_ge(b1t_ready, 1)
            with act.Fori(0, NE // 2) as i:
                act.wait_ge(h_ready, (i + 1) * (UN * FC) + FC)
                act.sem_inc(pair_begun, 1)
                act.activation(biasS[:, :], biasT[:, bass.ds(i * (2 * FC), 2 * FC)], ACT.Copy).then_inc(pair_bias, 1)
                act.wait_ge(pair_bias, i + 1)
                gelus(UN, i, biasS)

        @block.tensor
        def _(pe):
            def transpose_group(n):
                for g in range(NG):
                    pe.wait_ge(ln_ready, n * NG + g + 1)
                    if n * NG + g:
                        pe.wait_ge(xt_ready, 2 * (n * NG + g))
                    for k in range(2):
                        for b in range(GB):
                            c = (k * GB + b) * P
                            ins = pe.transpose(flat[:, c:c + P], XN[:, g * GB + b, k * P:(k + 1) * P], ident[:, :])
                    ins.then_inc(tr_ready, 1)

            for h in range(2):
                pe.sem_inc(ohb_used[h], 1)
                pe.sem_inc(step_used[h], 1)
            pe.wait_ge(consts, 10)
            transpose_group(0)
            pe.wait_ge(sel_ready, 1)
            pe.wait_ge(xt_ready, 2 * NG)
            for bank, rows_of in ((0, SF), (1, DF)):
                for c in range(EC):
                    pe.matmul(ps[:, bank, 0:STEPS], rows_of[:, c, :], S[:, c, :], start=(c == 0), stop=(c == EC - 1))
            for c in range(EC):
                ins = pe.matmul(ps[:, 2, 0:STEPS], tcol[:, c:c + 1].broadcast_to([P, P]), S[:, c, :], start=(c == 0), stop=(c == EC - 1))
            ins.then_inc(steps_ps, 1)
            pe.wait_ge(steps_ready, 1)
            for q in range(4):
                for bank, rows_of in ((4, SF), (5, DF)):
                    for c in range(EC):
                        pe.matmul(ps[0:KC, bank, q * P:(q + 1) * P], S[:, c, q * KC:(q + 1) * KC], rows_of[:, c, :], start=(c == 0), stop=(c == EC - 1))
                for c in range(EC):
                    ins = pe.matmul(ps[0:KC, 6, q:q + 1], S[:, c, q * KC:(q + 1) * KC], tcol[:, c:c + 1], start=(c == 0), stop=(c == EC - 1))
            ins.then_inc(rows_ps, 1)
            pe.wait_ge(dr_ready, 1)
            for e, bank in ((0, 0), (P - 1, 1)):
                for q in range(4):
                    ins = pe.transpose(ps[0:HEADS, bank, q * KC:(q + 1) * KC], DR[:, q, e:e + 1].broadcast_to([KC, HEADS]), ident[0:KC, 0:KC])
            ins.then_inc(ends_ps, 1)
            pe.wait_ge(f0_ready, 1)
            for q in range(4):
                ins = pe.transpose(ps[0:KC, 2, q * HEADS:(q + 1) * HEADS], lev[:, 0, q * KC:(q + 1) * KC], ident[0:HEADS, 0:HEADS])
            ins.then_inc(lf_ps, 1)
            pe.wait_ge(lfr_ready, 1)
            for q in range(4):
                ins = pe.transpose(ps[:, 0, q * KC:(q + 1) * KC], LFR[:, q, :], ident[0:KC, 0:KC])
            ins.then_inc(lft_ps, 1)
            pe.matmul(ps[:, 3, 0:NB], zeros[:, 0:P], zeros[:, 0:NB], start=True, stop=False)
            with pe.Fori(0, IT) as i:
                for h in range(2):
                    pe.wait_ge(ohb_ready[h], i * 2 + 2)
                    for s in range(HALF):
                        ins = pe.matmul(ps[:, 3, 0:NB], OHB[:, h, s, :], HSEL[:, h, s, :], start=False, stop=False)
                    ins.then_inc(ohb_used[h], 1)
            pe.matmul(ps[:, 3, 0:NB], zeros[:, 0:P], zeros[:, 0:NB], start=False, stop=True).then_inc(deg_ps, 1)
            pe.wait_ge(w_in, 64)
            for g in range(NG):
                if g:
                    pe.wait_ge(h1_ready, g)
                for b in range(GB):
                    for k in range(2):
                        ins = pe.matmul(flat[:, 2048 + b * P:2048 + (b + 1) * P], XT[:, k, (g * GB + b) * P:(g * GB + b + 1) * P], W1[:, k, :],
                                        start=(k == 0), stop=(k == 1))
                ins.then_inc(h1_ps, 1)

            def aggregate(n):
                pe.wait_ge(h1_ready, (n + 1) * NG)
                pe.wait_ge(prep_done, 1)
                for bank in range(7):
                    pe.matmul(ps[:, bank, :], zeros[:, 0:P], zeros[:, :], start=True, stop=False)
                regs = [pe.alloc_register(f"pe_blk{n}_{s}") for s in range(HALF)]
                with pe.Fori(0, IT) as i:
                    for h in range(2):
                        pe.load(regs, BLKI[0:1, bass.ds(i * (2 * HALF) + h * HALF, HALF)])
                        blks = [pe.snap(r, min_val=0, max_val=NB - 1) for r in regs]
                        pe.wait_ge(oh_ready[h], i + (n * IT + 1))
                        pe.wait_ge(gathered[h], (i + (n * IT + 1)) * (16 * HALF))
                        for s in range(HALF):
                            blk = blks[s]
                            ins = pe.matmul(acc[:, bass.ds(blk * HID, HID)], OH[:, h, s, :], ring[:, h, s, 0:HID],
                                            start=False, stop=False, skip_group_check=True)
                        ins.then_inc(step_used[h], 1)
                for bank in range(7):
                    ins = pe.matmul(ps[:, bank, :], zeros[:, 0:P], zeros[:, :], start=False, stop=True)
                ins.then_inc(agg_done, 1)

            aggregate(0)
            aggregate(1)
            for g in range(NG):
                if g == 0:
                    pe.wait_ge(agg_free, 2 * NG)
                if g:
                    pe.wait_ge(aggT_ready, g)
                for b in range(GB):
                    ins = pe.transpose(flat[:, b * P:(b + 1) * P], H[:, g * GB + b, 0:HID], ident[:, :])
                ins.then_inc(aggT_ps, 1)
                pe.wait_ge(aggT_ready, g + 1)
                if g:
                    pe.wait_ge(x_ready, g)
                for b in range(GB):
                    ins = pe.matmul(flat[:, 1024 + b * D:1024 + (b + 1) * D], XT[:, 0, (g * GB + b) * P:(g * GB + b + 1) * P], W2[:, :], start=True, stop=True)
                ins.then_inc(o_ps, 1)
            pe.wait_ge(x_ready, NG)
            transpose_group(1)
            pe.wait_ge(mean_ready, 1)
            pe.wait_ge(moe_in, 16 * 6)
            for k in range(2):
                ins = pe.matmul(ps[:, 4, 0:NE], mean[:, k:k + 1].broadcast_to([P, P]), Wr[:, k, :], start=(k == 0), stop=(k == 1))
            ins.then_inc(logits_ps, 1)
            pe.wait_ge(sel_out, 1)
            for f in range(FC):
                pe.matmul(ps[:, 5, 2 * f:2 * f + 2], b1rows[:, f * P:(f + 1) * P], sel[:, 0:2], start=True, stop=True)
            pe.matmul(ps[:, 6, 0:D], sel[:, 2:3].broadcast_to([NE, P]), b2rows[:, :], start=True, stop=True).then_inc(bias_ps, 1)

            def expert_products(base, i, weights):
                def second(u):
                    U = (0 if i is None else i * UN) + base + u
                    k, c = divmod(u, len(CH))
                    pe.wait_ge(h_ready, U * FC + 2 * FC)
                    pe.wait_ge(y_taken, U + 1)
                    if i is None and u == 1:
                        pe.wait_ge(target_ready, 1)
                    for b in range(CH[c]):
                        for f in range(FC):
                            o = (4 + 2 * (u % 2)) * 512 + b * D
                            ins = pe.matmul(flat[:, o:o + D], HT[:, u % 2, f, b * P:(b + 1) * P], W2E[:, k, f, :], start=(f == 0), stop=(f == FC - 1))
                    ins.then_inc(y_ps, 1)

                for u in range(UN):
                    U = (0 if i is None else i * UN) + base + u
                    k, c = divmod(u, len(CH))
                    if c == 0:
                        weights(k)
                    for f in range(FC):
                        pe.wait_ge(h_ready, U * FC + (f + 1))
                        for j in range(2):
                            ins = pe.matmul(ps[:, f, 0:CH[c] * P], W1E[:, k, j, f * P:(f + 1) * P], XT[:, j, C0[c] * P:(C0[c] + CH[c]) * P],
                                            start=(j == 0), stop=(j == 1))
                        ins.then_inc(h_ps, 1)
                    if u:
                        second(u - 1)
                second(UN - 1)

            pe.wait_ge(xt_ready, 4 * NG)
            pe.wait_ge(bias_ready, 1)
            pe.sem_inc(h_ready, FC)
            pe.sem_inc(y_ps, 2)
            pe.sem_inc(y_taken, 2)
            expert_products(0, None, lambda k: pe.wait_ge(w_ready[k], 32))
            for q in range(PARTS):
                pe.sem_inc(slot_used[q], 1)
            transpose_group(2)
            pe.wait_ge(xt_ready, 6 * NG)
            pe.wait_ge(wg_ready, 1)
            for c in range(len(CH)):
                if c >= 2:
                    pe.wait_ge(h3_ready, 2 * (c - 1))
                for b in range(CH[c]):
                    for k in range(2):
                        ins = pe.matmul(ps[:, 4 * (c % 2) + b, 0:ROW], XT[:, k, (C0[c] + b) * P:(C0[c] + b + 1) * P], WG[:, k, :], start=(k == 0), stop=(k == 1))
                ins.then_inc(h3_ps, 1)
            pe.wait_ge(h3_ready, 2 * len(CH))
            pe.wait_ge(split_ready, 1)
            for h in range(2):
                for s_ in (look_ps[h], v_taken[h], ad_taken[h]):
                    pe.sem_inc(s_, 1)
            regs = [pe.alloc_register(f"pe_look{s}") for s in range(HALF)]

            def lookups(i, sources):
                for h in range(2):
                    pe.load(regs, BLKI[0:1, bass.ds(i * (2 * HALF) + h * HALF, HALF)])
                    blks = [pe.snap(r, min_val=0, max_val=NB - 1) for r in regs]
                    pe.wait_ge(ot_ready[h], i * 2 + 3)
                    if sources:
                        pe.wait_ge(v_taken[h], i + 1)
                    pe.wait_ge(ad_taken[h], i + 1)
                    for s in range(HALF):
                        if sources:
                            for n in range(3):
                                pe.matmul(ps[:, 2 * h + s // 4, (s % 4) * NB * HEADS:(s % 4 + 1) * NB * HEADS], OTS[:, h, s * P:(s + 1) * P],
                                          A8P[:, :, n, 0:HEADS], start=(n == 0), stop=(n == 2))
                        ins = pe.matmul(ps[:, 4 + h, s * 6 * HEADS:(s + 1) * 6 * HEADS], OTD[:, h, s * P:(s + 1) * P],
                                        A8P[:, :, :, :].rearrange("p b n m -> p (b n m)")[:, bass.ds(blks[s] * (6 * HEADS), 6 * HEADS)], start=True, stop=True)
                    ins.then_inc(look_ps[h], 1)

            with pe.Fori(0, LOOK) as i:
                lookups(i, True)
            with pe.Fori(LOOK, IT) as i:
                lookups(i, False)
            pe.wait_ge(v_ready, 1)
            for h in range(2):
                pe.wait_ge(va_out[h], IT - LOOK)
            for h in range(2):
                pe.wait_ge(ad_taken[h], IT + 1)
            for q in range(4):
                for n in range(HEADS):
                    ins = pe.transpose(ps[0:KC, q, n * P:(n + 1) * P], V[:, q * KC:(q + 1) * KC, n], ident[:, :])
            ins.then_inc(vrow_ps, 1)
            pe.wait_ge(ends_ready, 1)
            for d in range(2):
                for q in range(4):
                    ins = pe.transpose(ps[0:HEADS, 4 + d, q * KC:(q + 1) * KC], ends[:, d, q, :], ident[0:KC, 0:KC])
            ins.then_inc(lev_ps, 1)
            pe.wait_ge(car_ready, 1)
            for d in range(2):
                for q in range(4):
                    o = (d * 4 + q) * HEADS
                    ins = pe.transpose(ps[0:KC, 6, o:o + HEADS], car[:, d, q * KC:(q + 1) * KC], ident[0:HEADS, 0:HEADS])
            ins.then_inc(cin_ps, 1)
            pe.wait_ge(max_ready, 1)
            for n in range(HEADS):
                for q in range(4):
                    ins = pe.transpose(ps[:, 4 + n, q * KC:(q + 1) * KC], SCF[:, q, n, :], ident[0:KC, 0:KC])
            ins.then_inc(max_ps, 1)
            pe.wait_ge(gap_ready, 1)
            for q in range(2):
                pe.sem_inc(quad_taken, 1)
            with pe.Fori(0, IT) as i:
                for q in range(PARTS):
                    pe.wait_ge(slot_msg[q], i * 2 + 2)
                    pe.wait_ge(slot_oh[q], i + 1)
                    pe.wait_ge(quad_taken, i * PARTS + (q + 1))
                    for s in range(PS):
                        ins = pe.matmul(ps[:, PS * (q % 2) + s, 0:ROW], OH4[:, q, s, :], RING4[:, q, s, :], start=True, stop=True)
                    ins.then_inc(slot_used[q], 1)

            transpose_group(3)
            pe.wait_ge(xt_ready, 8 * NG)
            pe.wait_ge(gate_in, 64)
            for b in range(NB):
                for k in range(2):
                    ins = pe.matmul(ps[:, 3, b * NE:(b + 1) * NE], XT[:, k, b * P:(b + 1) * P], gate[:, k, :], start=(k == 0), stop=(k == 1))
            ins.then_inc(gate_ps, 1)
            pe.transpose(ps[:, 7, 0:NE * FC], b1r32[:, :], ident[0:NE * FC, 0:NE * FC]).then_inc(b1t_ps, 1)
            pe.wait_ge(cw_ready, 1)
            for c in range(len(CH)):
                for b in range(CH[c]):
                    ins = pe.transpose(ps[0:NE, c, b * P:(b + 1) * P], CW[:, C0[c] + b, :], ident[:, :])
                ins.then_inc(cwt_ps, 1)
            pe.wait_ge(cwt_ready, len(CH))
            pe.wait_ge(b1t_ready, 1)
            for c in range(len(CH)):
                if c >= 2:
                    pe.wait_ge(b2_taken, c - 1)
                for b in range(CH[c]):
                    o = (4 + 2 * (c % 2)) * 512 + b * D
                    ins = pe.matmul(flat[:, o:o + D], CWT[:, (C0[c] + b) * P:(C0[c] + b + 1) * P], b2rows2[:, :], start=True, stop=True)
                ins.then_inc(b2_ps, 1)
            pe.wait_ge(b2_taken, len(CH))
            with pe.Fori(0, NE // 2) as i:
                expert_products(UN, i, lambda k: pe.wait_ge(w_ready[k], i * 32 + 64))

        @block.vector
        def _(dve):
            ch = Chain(dve, dve_op)

            def layer_norm(n, std, loaded=lambda g: None):
                for g in range(NG):
                    loaded(g)
                    for b in range(g * GB, (g + 1) * GB):
                        ch.mark(dve.bn_stats(stats[:, b, :], X[:, b, :]))
                dve.wait_ge(dve_op, ch.value())
                for b in range(NB):
                    ins = dve.bn_aggr(mv[:, b, :], stats[:, b, :])
                    if b < NB - 1:
                        ch.mark(ins)
                ins.then_inc(var_ready, 1)
                dve.wait_ge(std_ready, std + 1)
                ch.link(dve.reciprocal(rstd[:, :], rstd[:, :]))
                for g in range(NG):
                    for b in range(GB):
                        ins = dve.tensor_scalar(XN[:, g * GB + b, :], X[:, g * GB + b, :], mv[:, g * GB + b, 0:1], rstd[:, g * GB + b:g * GB + b + 1],
                                                ALU.subtract, ALU.mult)
                        if b < GB - 1:
                            ch.mark(ins)
                    ins.then_inc(ln_ready, 1)

            def x_loaded(g):
                if g == NG - 1:
                    dve.wait_ge(x_in[g], 32)
                else:
                    dve.wait_ge(x_in[g], 16)

            dve.wait_ge(pads, 5)
            layer_norm(0, 0, x_loaded)
            dve.wait_ge(edges_in, 16 * (6 + EC))
            dve.wait_ge(consts, 10)
            ch.mark(dve.tensor_scalar(ELI[:, :], DI[:, :, P - 1], 7, None, ALU.arith_shift_right))
            ch.link(dve.tensor_scalar(EPI[:, :], EPI[:, :], 7, None, ALU.arith_shift_right))
            ch.mark(dve.tensor_tensor(thi[:, :], ELI[:, :], tcol[:, :], ALU.add))
            ch.mark(dve.tensor_tensor(tlo[:, :], EPI[:, :], tcol[:, :], ALU.add))
            ch.mark(dve.tensor_copy(SF[:, :, :], SI[:, :, :]))
            ch.link(dve.tensor_copy(DF[:, :, :], DI[:, :, :]))
            for c in range(EC):
                ch.mark(dve.tensor_scalar(S[:, c, :], iotaK[:, :], tlo[:, c:c + 1], None, ALU.is_ge))
            dve.wait_ge(dve_op, ch.value())
            for c in range(EC):
                ins = dve.scalar_tensor_tensor(S[:, c, :], iotaK[:, :], thi[:, c:c + 1], S[:, c, :], ALU.is_le, ALU.mult)
                if c < EC - 1:
                    ch.mark(ins)
            ins.then_inc(sel_ready, 1)
            dve.wait_ge(steps_ps, 1)
            ch.mark(dve.tensor_tensor(BLKI[:, :], iotaK[:, :], ps[:, 2, 0:STEPS], ALU.subtract))
            ch.mark(dve.tensor_copy(IDX[:, :], ps[:, 0, 0:STEPS]))
            ch.link(dve.tensor_tensor(BLKF[:, :], iotaK[:, :], ps[:, 2, 0:STEPS], ALU.subtract))
            ch.link(dve.scalar_tensor_tensor(DLOC[:, :], BLKF[:, :], -float(P), ps[:, 1, 0:STEPS], ALU.mult, ALU.add))
            dve.nop().then_inc(steps_ready, 1)
            ch.link(dve.tensor_scalar(BLKI2[:, :], IDX[:, :], 7, None, ALU.arith_shift_right))
            ch.mark(dve.tensor_copy(SHI[:, :], BLKI2[:, :]))
            dve.wait_ge(rows_ps, 1)
            ch.mark(dve.tensor_copy(DR[:, :, :], ps[0:KC, 5, :].rearrange("p (c e) -> p c e", e=P)))
            ch.mark(dve.tensor_copy(SRI[:, :, :], ps[0:KC, 4, :].rearrange("p (c e) -> p c e", e=P)))
            ch.link(dve.tensor_tensor(bcol[:, :], krow[:, :], ps[0:KC, 6, 0:4], ALU.subtract))
            dve.nop().then_inc(dr_ready, 1)
            ch.mark(dve.tensor_scalar(SRI[:, :, :], SRI[:, :, :], P - 1, None, ALU.bitwise_and))
            ch.link(dve.tensor_scalar(bcol[:, :], bcol[:, :], -float(P), None, ALU.mult))
            dve.tensor_copy(lowS[:, :, :], SRI[:, :, :]).then_inc(low_ready, 1)
            dve.tensor_tensor(lowD[:, :, :], DR[:, :, :], bcol[:, :].unsqueeze(2).broadcast_to([KC, 4, P]), ALU.add).then_inc(low_ready, 1)
            ch.link(dve.tensor_tensor(LFR[:, :, 0:P - 1], DR[:, :, 1:P], DR[:, :, 0:P - 1], ALU.not_equal))
            ch.mark(dve.tensor_scalar(NFX[:, :, 1:P], LFR[:, :, 0:P - 1], -BIG, None, ALU.mult))
            dve.wait_ge(ends_ps, 1)
            ch.mark(dve.tensor_copy(lev[:, 0, :], ps[0:HEADS, 0, 0:STEPS]))
            ch.link(dve.tensor_copy(lev[:, 1, :], ps[0:HEADS, 1, 0:STEPS]))
            ch.mark(dve.memset(newF[:, 0:1], 1.0))
            ch.mark(dve.tensor_tensor(newF[:, 1:STEPS], lev[:, 0, 1:STEPS], lev[:, 1, 0:STEPS - 1], ALU.not_equal))
            ch.link(dve.tensor_tensor(car[:, 0, :], lev[:, 0, :], lev[:, 1, :], ALU.not_equal))
            ch.mark(dve.memset(lev[:, 0, STEPS - 1:STEPS], 1.0))
            ch.mark(dve.tensor_copy(lev[:, 0, 0:STEPS - 1], newF[:, 1:STEPS]))
            ch.link(dve.tensor_tensor(brkF[:, :], newF[:, :], car[:, 0, :], ALU.max))
            dve.nop().then_inc(f0_ready, 1)
            ch.link(dve.tensor_tensor(brkB[:, :], lev[:, 0, :], car[:, 0, :], ALU.max))
            for flag in (brkF, brkB, newF):
                ins = ch.mark(dve.tensor_scalar(flag[:, :], flag[:, :], -BIG, None, ALU.mult))
            dve.wait_ge(lf_ps, 1)
            ch.link(dve.tensor_copy(lf127[:, :, :], ps[0:KC, 2, 0:4 * HEADS].rearrange("p (c n) -> p c n", n=HEADS)))
            dve.tensor_copy(LFR[:, :, P - 1:P], lf127[:, :, 0:1]).then_inc(lfr_ready, 1)
            dve.wait_ge(lft_ps, 1)
            dve.tensor_copy(LFT[:, :], ps[:, 0, 0:STEPS]).then_inc(prep_done, 1)
            with dve.Fori(0, IT) as i:
                for h in range(2):
                    k = i * (2 * HALF) + h * HALF
                    dve.wait_ge(ohb_used[h], i + 1)
                    dve.tensor_tensor(HSEL[:, h, :, :], iotaK[:, 0:NB].unsqueeze(1).broadcast_to([P, HALF, NB]),
                                      BLKF[:, bass.ds(k, HALF)].unsqueeze(2).broadcast_to([P, HALF, NB]), ALU.is_equal).then_inc(ohb_ready[h], 1)
                    dve.tensor_tensor(OHB[:, h, :, :], iotaK[:, 0:P].unsqueeze(1).broadcast_to([P, HALF, P]),
                                      DLOC[:, bass.ds(k, HALF)].unsqueeze(2).broadcast_to([P, HALF, P]), ALU.is_equal).then_inc(ohb_ready[h], 1)
            dve.wait_ge(deg_root, 1)
            ch.link(dve.reciprocal(dinv[:, :], dinv[:, :]))
            for g in range(NG):
                dve.wait_ge(h1_ps, g + 1)
                dve.tensor_tensor(H[:, g * GB:(g + 1) * GB, 0:HID], flat[:, 2048:2048 + GB * P].rearrange("p (b n) -> p b n", b=GB),
                                  dinv[:, g * GB:(g + 1) * GB].unsqueeze(2).broadcast_to([P, GB, HID]), ALU.mult).then_inc(h1_ready, 1)

            def one_hots(n):
                with dve.Fori(0, IT) as i:
                    for h in range(2):
                        k = i * (2 * HALF) + h * HALF
                        dve.wait_ge(step_used[h], i + (n * IT + 1))
                        dve.tensor_tensor(OH[:, h, :, :], iotaK[:, 0:P].unsqueeze(1).broadcast_to([P, HALF, P]),
                                          DLOC[:, bass.ds(k, HALF)].unsqueeze(2).broadcast_to([P, HALF, P]), ALU.is_equal).then_inc(oh_ready[h], 1)

            one_hots(0)
            dve.wait_ge(w_in, 64)
            dve.wait_ge(t_out, 16 * NG)
            dve.wait_ge(agg_done, 1)
            for g in range(NG):
                hg = H[:, g * GB:(g + 1) * GB, 0:HID]
                ag = acc[:, g * GB * HID:(g + 1) * GB * HID].rearrange("p (b n) -> p b n", b=GB)
                dg = dinv[:, g * GB:(g + 1) * GB].unsqueeze(2).broadcast_to([P, GB, HID])
                ch.link(dve.tensor_tensor(hg, hg, ag, ALU.add))
                ch.link(dve.tensor_tensor(hg, hg, dg, ALU.mult))
                ch.link(dve.tensor_tensor(hg, hg, b1bc[:, :].unsqueeze(1).broadcast_to([P, GB, HID]), ALU.add))
                dve.scalar_tensor_tensor(hg, hg, 0.0, dg, ALU.max, ALU.mult).then_inc(h1_ready, 1)
            dve.wait_ge(h1_ready, 2 * NG)
            one_hots(1)
            for g in range(NG):
                xg = X[:, g * GB:(g + 1) * GB, :]
                ch.link(dve.tensor_tensor(xg, xg, b2bc[:, :].unsqueeze(1).broadcast_to([P, GB, D]), ALU.add))
            dve.wait_ge(t_out, 32 * NG)
            dve.wait_ge(agg_done, 2)
            for g in range(NG):
                hg = H[:, g * GB:(g + 1) * GB, 0:HID]
                ag = acc[:, g * GB * HID:(g + 1) * GB * HID].rearrange("p (b n) -> p b n", b=GB)
                dg = dinv[:, g * GB:(g + 1) * GB].unsqueeze(2).broadcast_to([P, GB, HID])
                ch.link(dve.tensor_tensor(hg, hg, ag, ALU.add))
                dve.tensor_tensor(hg, hg, dg, ALU.mult).then_inc(agg_free, 1 if g else NG + 1)
            for g in range(NG):
                dve.wait_ge(o_ps, g + 1)
                xg = X[:, g * GB:(g + 1) * GB, :]
                dve.tensor_tensor(xg, xg, flat[:, 1024:1024 + GB * D].rearrange("p (b n) -> p b n", b=GB), ALU.add).then_inc(x_ready, 1)
            dve.wait_ge(x_ready, NG)
            layer_norm(1, 1)
            dve.wait_ge(xt_ready, 4 * NG)
            ch.link(dve.tensor_reduce(mean[:, :], msum[:, :, :], AX.X, ALU.add))
            dve.tensor_scalar(mean[:, :], mean[:, :], 1.0 / N, None, ALU.mult).then_inc(mean_ready, 1)
            dve.wait_ge(logits_ps, 1)

            def softmax(n, w):
                ch.link(dve.tensor_reduce(rs[:, 12:13], rt[:, 2 * n, 0:w], AX.X, ALU.max))
                dve.tensor_scalar(rs[:, n:n + 1], rs[:, 12:13], -1.0, None, ALU.mult).then_inc(exp_in, 1)
                dve.wait_ge(exp_out, n + 1)
                ch.link(dve.reciprocal(rs[:, 8 + n:9 + n], rs[:, 4 + n:5 + n]))
                ch.link(dve.tensor_scalar(rt[:, 2 * n + 1, 0:w], rt[:, 2 * n + 1, 0:w], rs[:, 8 + n:9 + n], None, ALU.mult))

            ch.link(dve.tensor_tensor(rt[:, 0, :], ps[:, 4, 0:NE], brbc[:, :], ALU.add))
            softmax(0, NE)
            ch.link(dve.tensor_scalar(rt[:, 6, :], rt[:, 1, :], float(N), None, ALU.mult))
            ch.link(dve.reciprocal(rt[:, 7, :], rt[:, 6, :]))
            ch.link(dve.tensor_scalar(rt[:, 7, :], rt[:, 7, :], CAP, 1.0, ALU.mult, ALU.min))
            ch.link(dve.tensor_tensor(rt[:, 2, :], rt[:, 1, :], rt[:, 7, :], ALU.mult))
            softmax(1, NE)
            ch.link(dve.max(rt[:, 4, :], rt[:, 3, :]))
            ch.link(dve.max_index(topi[:, :], rt[:, 4, :], rt[:, 3, :]))
            dve.nop().then_inc(route_done, 1)
            ch.link(dve.tensor_copy(topf[:, :], topi[:, :]))
            softmax(2, 2)
            ch.link(dve.tensor_scalar(sel[:, 0:2], topf[0:NE, 0:2], iotaP[0:NE, 0:1], None, ALU.is_equal))
            ch.link(dve.tensor_tensor(rs[0:NE, 13:15], sel[:, 0:2], rt[0:NE, 5, 0:2], ALU.mult))
            dve.tensor_tensor(sel[:, 2:3], rs[0:NE, 13:14], rs[0:NE, 14:15], ALU.add).then_inc(sel_out, 1)
            dve.wait_ge(bias_ps, 1)
            dve.tensor_copy(biasT[:, 0:2 * FC].rearrange("p (k f) -> p k f", k=2), ps[:, 5, 0:2 * FC].rearrange("p (f k) -> p k f", k=2)).then_inc(bias_ready, 1)
            for g in range(NG):
                ch.mark(dve.tensor_tensor(H[:, g * GB:(g + 1) * GB, :], XN[:, g * GB:(g + 1) * GB, :],
                                          ps[:, 6, 0:D].unsqueeze(1).broadcast_to([P, GB, D]), ALU.add))
            dve.wait_ge(dve_op, ch.value())
            dve.nop().then_inc(target_ready, 1)

            for g in range(NG):
                xg = X[:, g * GB:(g + 1) * GB, :]
                ch.mark(dve.tensor_tensor(xg, xg, betbc[:, :].unsqueeze(1).broadcast_to([P, GB, D]), ALU.add))
            dve.wait_ge(dve_op, ch.value())

            def add_experts(base, i, target, weight):
                for u in range(UN):
                    U = (0 if i is None else i * UN) + base + u
                    k, c = divmod(u, len(CH))
                    dve.wait_ge(y_ps, U + 3)
                    if u >= len(CH) or i is not None:
                        dve.wait_ge(y_taken, U + (3 - len(CH)))
                    for b in range(CH[c]):
                        o = (4 + 2 * (u % 2)) * 512 + b * D
                        t = target[:, C0[c] + b, :]
                        ins = dve.scalar_tensor_tensor(t, flat[:, o:o + D], weight(k, C0[c] + b), t, ALU.mult, ALU.add)
                        if b < CH[c] - 1:
                            ch.mark(ins)
                    ins.then_inc(y_taken, 1)

            dve.wait_ge(target_ready, 1)
            add_experts(0, None, H, lambda k, b: rt[:, 5, k:k + 1])
            dve.wait_ge(y_taken, UN + 2)
            for b in range(NB):
                ch.mark(dve.bn_stats(stats[:, b, :], H[:, b, :]))
            dve.wait_ge(dve_op, ch.value())
            for b in range(NB):
                ins = dve.bn_aggr(mv[:, b, :], stats[:, b, :])
                if b < NB - 1:
                    ch.mark(ins)
            ins.then_inc(var_ready, 1)
            dve.wait_ge(std_ready, 3)
            ch.link(dve.reciprocal(rstd[:, :], rstd[:, :]))
            for g in range(NG):
                for b in range(g * GB, (g + 1) * GB):
                    ch.mark(dve.tensor_scalar(H[:, b, :], H[:, b, :], mv[:, b, 0:1], rstd[:, b:b + 1], ALU.subtract, ALU.mult))
                dve.wait_ge(dve_op, ch.value())
                hg, xg = H[:, g * GB:(g + 1) * GB, :], X[:, g * GB:(g + 1) * GB, :]
                ch.link(dve.tensor_tensor(hg, hg, gambc[:, :].unsqueeze(1).broadcast_to([P, GB, D]), ALU.mult))
                dve.tensor_tensor(xg, xg, hg, ALU.add).then_inc(x_ready, 1)
            dve.wait_ge(x_ready, 2 * NG)
            layer_norm(2, 3)
            dve.wait_ge(att_in, 64)
            for n in range(2):
                ch.link(dve.tensor_tensor(WA[:, :, :], WG[:, :, 0:D], attbc[:, n:n + 1, :].broadcast_to([P, 2, D]), ALU.mult))
                ch.link(dve.tensor_reduce(WG[:, :, D + n * HEADS:D + (n + 1) * HEADS], WA[:, :, :].rearrange("p k (h c) -> p k h c", c=HC), AX.X, ALU.add))
            dve.nop().then_inc(wg_ready, 1)
            dve.wait_ge(h3_ready, 2 * len(CH))
            ch.link(dve.tensor_copy(A8P[:, :, 0, :], A8[:, :, :]))
            ch.link(dve.tensor_tensor(A8R[:, :, :], A8[:, :, :], A8P[:, :, 0, :], ALU.subtract))
            ch.link(dve.tensor_copy(A8P[:, :, 1, :], A8R[:, :, :]))
            ch.link(dve.tensor_tensor(A8R[:, :, :], A8R[:, :, :], A8P[:, :, 1, :], ALU.subtract))
            dve.tensor_copy(A8P[:, :, 2, :], A8R[:, :, :]).then_inc(split_ready, 1)
            for h in range(2):
                dve.sem_inc(ot_ready[h], 1)

            def compare(i, h):
                k = i * (2 * HALF) + h * HALF
                dve.wait_ge(br_in[h], i * 32 + 32)
                dve.wait_ge(look_ps[h], i + 1)
                dve.tensor_scalar(OTS[:, h, :], BRS[:, h, :], iotaP[:, 0:1], None, ALU.is_equal).then_inc(ot_ready[h], 1)
                dve.tensor_scalar(OTD[:, h, :], BRD[:, h, :], iotaP[:, 0:1], None, ALU.is_equal).then_inc(ot_ready[h], 1)
                dve.wait_ge(v_taken[h], i + 1)
                dve.tensor_tensor(MSK[:, h, :].rearrange("p (k n) -> p k n", n=NB), iotaK[:, 0:NB].unsqueeze(1).broadcast_to([P, HALF, NB]),
                                  SHI[:, bass.ds(k, HALF)].unsqueeze(2).broadcast_to([P, HALF, NB]), ALU.is_equal).then_inc(msk_ready[h], 1)

            def select(i, h):
                k = i * (2 * HALF) + h * HALF
                dve.wait_ge(msk_ready[h], i + 1)
                dve.wait_ge(look_ps[h], i + 2)
                dve.tensor_tensor(SELV[:, h, :, :].rearrange("p (g m) n -> p g m n", g=2),
                                  ps[:, 2 * h:2 * h + 2, 0:4 * NB * HEADS].rearrange("p g (m n) -> p g m n", n=HEADS),
                                  MSK[:, h, :].rearrange("p (g m) -> p g m", g=2).unsqueeze(3).broadcast_to([P, 2, 4 * NB, HEADS]), ALU.mult).then_inc(v_taken[h], 1)
                dve.tensor_reduce(AD[:, bass.ds(k, HALF), :], ps[:, 4 + h, 0:HALF * 6 * HEADS].rearrange("p (k n m) -> p k m n", n=3, m=2 * HEADS),
                                  AX.X, ALU.add).then_inc(ad_taken[h], 1)
                dve.wait_ge(v_taken[h], i + 2)
                ch.mark(dve.tensor_reduce(V[:, bass.ds(k, HALF), :], SELV[:, h, :, :].rearrange("p (k m) n -> p k n m", k=HALF), AX.X, ALU.add))

            def compare_dst(i, h):
                dve.wait_ge(br_in[h], i * 16 + (16 * LOOK + 16))
                dve.wait_ge(look_ps[h], i + 1)
                dve.tensor_scalar(OTD[:, h, :], BRD[:, h, :], iotaP[:, 0:1], None, ALU.is_equal).then_inc(ot_ready[h], 2)

            def select_dst(i, h):
                dve.wait_ge(look_ps[h], i + 2)
                dve.tensor_reduce(AD[:, bass.ds(i * (2 * HALF) + h * HALF, HALF), :], ps[:, 4 + h, 0:HALF * 6 * HEADS].rearrange("p (k n m) -> p k m n", n=3, m=2 * HEADS),
                                  AX.X, ALU.add).then_inc(ad_taken[h], 1)

            compare(0, 0)
            with dve.Fori(0, LOOK - 1) as i:
                ch.enter(i, 2)
                compare(i, 1)
                select(i, 0)
                compare(i + 1, 0)
                select(i, 1)
                ch.leave(LOOK - 1)
            compare(LOOK - 1, 1)
            select(LOOK - 1, 0)
            select(LOOK - 1, 1)
            compare_dst(LOOK, 0)
            with dve.Fori(LOOK, IT - 1) as i:
                compare_dst(i, 1)
                select_dst(i, 0)
                compare_dst(i + 1, 0)
                select_dst(i, 1)
            compare_dst(IT - 1, 1)
            select_dst(IT - 1, 0)
            select_dst(IT - 1, 1)
            dve.wait_ge(dve_op, ch.value())
            dve.nop().then_inc(v_ready, 1)
            for h in range(2):
                dve.wait_ge(ad_taken[h], IT + 1)
                dve.wait_ge(va_out[h], IT - LOOK)
            dve.wait_ge(vrow_ps, 1)
            scans = ((SCF, 0), (SCB, 1))

            def scan_steps(initial):
                for out_, d in scans:
                    for q in range(4):
                        for n in range(HEADS):
                            o, v = out_[:, q, n, :], ps[0:KC, q, n * P:(n + 1) * P]
                            if d == 0:
                                flags = NFX[:, q, 0:P]
                            else:
                                flags, o, v = NFX[:, q, P:0:-1], out_[:, q, n, ::-1], ps[0:KC, q, (n + 1) * P - 1:(n * P - 1 if n else None):-1]
                            ch.mark(dve.tensor_tensor_scan(o, flags, v, initial(d, q, n), ALU.add, ALU.max))
                dve.wait_ge(dve_op, ch.value())

            scan_steps(lambda d, q, n: -BIG)
            ch.mark(dve.tensor_copy(ends[:, 0, :, :], SCF[:, :, :, P - 1]))
            ch.link(dve.tensor_copy(ends[:, 1, :, :], SCB[:, :, :, 0]))
            dve.nop().then_inc(ends_ready, 1)
            dve.wait_ge(lev_ps, 1)
            ch.mark(dve.tensor_tensor_scan(lev[:, 0, :], brkF[:, :], ps[0:HEADS, 4, 0:STEPS], -BIG, ALU.add, ALU.max))
            ch.mark(dve.tensor_tensor_scan(lev[:, 1, ::-1], brkB[:, ::-1], ps[0:HEADS, 5, STEPS - 1::-1], -BIG, ALU.add, ALU.max))
            ch.mark(dve.memset(car[:, 0, 0:1], -BIG))
            ch.link(dve.memset(car[:, 1, STEPS - 1:STEPS], -BIG))
            ch.mark(dve.tensor_tensor(car[:, 0, 1:STEPS], lev[:, 0, 0:STEPS - 1], newF[:, 1:STEPS], ALU.add))
            ch.link(dve.tensor_tensor(car[:, 1, 0:STEPS - 1], lev[:, 1, 1:STEPS], newF[:, 1:STEPS], ALU.add))
            dve.nop().then_inc(car_ready, 1)
            dve.wait_ge(cin_ps, 1)
            ch.link(dve.tensor_copy(cin[:, :, :, :].rearrange("p d q n -> p (d q n)"), ps[0:KC, 6, 0:8 * HEADS]))
            scan_steps(lambda d, q, n: cin[:, d, q, n:n + 1])
            dve.tensor_tensor(SCF[:, :, :, :], SCF[:, :, :, :], SCB[:, :, :, :], ALU.max).then_inc(max_ready, 1)
            dve.wait_ge(max_ps, 1)
            mx = ps[:, 4:8, 0:STEPS].rearrange("p n k -> p k n")
            a_s, a_d = AD[:, :, 0:HEADS], AD[:, :, HEADS:2 * HEADS]
            ch.mark(dve.tensor_tensor(PG[:, :, HEADS:2 * HEADS], mx, LFT[:, :].unsqueeze(2).broadcast_to([P, STEPS, HEADS]), ALU.mult))
            ch.mark(dve.tensor_tensor(V[:, :, :], V[:, :, :], a_d, ALU.add))
            ch.link(dve.tensor_tensor(a_s, mx, a_s, ALU.max))
            ch.link(dve.tensor_tensor(a_s, a_s, a_d, ALU.add))
            ch.mark(dve.scalar_tensor_tensor(V[:, :, :], V[:, :, :], SLOPE, V[:, :, :], ALU.mult, ALU.max))
            ch.link(dve.scalar_tensor_tensor(a_s, a_s, SLOPE, a_s, ALU.mult, ALU.max))
            ch.link(dve.tensor_tensor(V[:, :, :], V[:, :, :], a_s, ALU.subtract))
            dve.nop().then_inc(gap_ready, 1)
            ch.link(dve.memset(ACC[:, :, :], 0.0))
            dve.wait_ge(pg_ready, 1)

            def messages(i, q):
                k = i * (PARTS * PS) + q * PS
                dve.wait_ge(slot_used[q], i + 1)
                dve.tensor_tensor(OH4[:, q, :, :], iotaK[:, 0:P].unsqueeze(1).broadcast_to([P, PS, P]),
                                  DLOC[:, bass.ds(k, PS)].unsqueeze(2).broadcast_to([P, PS, P]), ALU.is_equal).then_inc(slot_oh[q], 1)
                dve.wait_ge(slot_in[q], (i + 1) * (16 * PS))
                m = RING4[:, q, :, 0:D].rearrange("p k (n c) -> p k n c", c=HC)
                dve.tensor_tensor(m, m, PG[:, bass.ds(k, PS), 0:HEADS].unsqueeze(3).broadcast_to([P, PS, HEADS, HC]), ALU.mult).then_inc(slot_msg[q], 1)
                dve.tensor_copy(RING4[:, q, :, D:ROW], PG[:, bass.ds(k, PS), :]).then_inc(slot_msg[q], 1)

            regs = [dve.alloc_register(f"dve_blk{s}") for s in range(PS)]
            accf = XTF[:, :]

            def add_steps(i, q):
                dve.load(regs, BLKI[0:1, bass.ds(i * (PARTS * PS) + q * PS, PS)])
                blks = [dve.snap(r, min_val=0, max_val=NB - 1) for r in regs]
                dve.wait_ge(slot_used[q], i + 2)
                for s in range(PS):
                    t = accf[:, bass.ds(blks[s] * ROW, ROW)]
                    ins = dve.tensor_tensor(t, t, ps[:, PS * (q % 2) + s, 0:ROW], ALU.add)
                    if s == PS - 1:
                        ins.then_inc(quad_taken, 1)
                        dve.wait_ge(quad_taken, i * PARTS + (q + 3))
                    else:
                        ch.link(ins)

            messages(0, 0)
            messages(0, 1)
            with dve.Fori(0, IT - 1) as i:
                ch.enter(i, PARTS * (PS - 1))
                for q in range(PARTS):
                    messages(i + (q + 2) // PARTS, (q + 2) % PARTS)
                    add_steps(i, q)
                ch.leave(IT - 1)
            for q in range(PARTS):
                if q + 2 < PARTS:
                    messages(IT - 1, q + 2)
                add_steps(IT - 1, q)
            an_s, an_d = A8[:, :, 0:HEADS], A8[:, :, HEADS:2 * HEADS]
            ch.link(dve.tensor_scalar(rstd[:, :], dinv[:, :], 0.9, -BIG, ALU.is_ge, ALU.mult))
            ch.link(dve.tensor_tensor(node[:, 0, :, :], ACC[:, :, D + HEADS:ROW], rstd[:, :].unsqueeze(2).broadcast_to([P, NB, HEADS]), ALU.add))
            ch.link(dve.tensor_tensor(node[:, 0, :, :], node[:, 0, :, :], an_s, ALU.max))
            ch.mark(dve.tensor_tensor(node[:, 1, :, :], an_s, an_d, ALU.add))
            ch.link(dve.tensor_tensor(node[:, 0, :, :], node[:, 0, :, :], an_d, ALU.add))
            for n in range(2):
                ch.mark(dve.scalar_tensor_tensor(node[:, n, :, :], node[:, n, :, :], SLOPE, node[:, n, :, :], ALU.mult, ALU.max))
            dve.wait_ge(dve_op, ch.value())
            dve.tensor_tensor(node[:, 2, :, :], node[:, 1, :, :], node[:, 0, :, :], ALU.subtract).then_inc(self_in, 1)
            dve.wait_ge(self_out, 1)
            ch.link(dve.tensor_tensor(node[:, 4, :, :], node[:, 3, :, :], ACC[:, :, D:D + HEADS], ALU.add))
            ch.link(dve.tensor_scalar(node[:, 4, :, :], node[:, 4, :, :], 1e-16, None, ALU.add))
            ch.link(dve.reciprocal(node[:, 4, :, :], node[:, 4, :, :]))
            for g in range(NG):
                gs = slice(g * GB, (g + 1) * GB)
                hg = H[:, gs, :].rearrange("p b (n c) -> p b n c", c=HC)
                ag = ACC[:, gs, 0:D].rearrange("p b (n c) -> p b n c", c=HC)
                ch.link(dve.tensor_tensor(hg, hg, node[:, 3, gs, :].unsqueeze(3).broadcast_to([P, GB, HEADS, HC]), ALU.mult))
                ch.link(dve.tensor_tensor(hg, hg, ag, ALU.add))
                ch.link(dve.tensor_tensor(hg, hg, node[:, 4, gs, :].unsqueeze(3).broadcast_to([P, GB, HEADS, HC]), ALU.mult))
                ch.link(dve.tensor_tensor(H[:, gs, :], H[:, gs, :], biasbc[:, :].unsqueeze(1).broadcast_to([P, GB, D]), ALU.add))
                dve.scalar_tensor_tensor(X[:, gs, :], H[:, gs, :], 0.0, X[:, gs, :], ALU.max, ALU.add).then_inc(x_ready, 1)
            dve.wait_ge(x_ready, 3 * NG)
            layer_norm(3, 4)
            dve.wait_ge(gate_ps, 1)
            ch.link(dve.tensor_tensor(CW[:, :, :], ps[:, 3, 0:NB * NE].rearrange("p (b e) -> p b e", e=NE), gbbc[:, :].unsqueeze(1).broadcast_to([P, NB, NE]), ALU.add))
            ch.link(dve.tensor_reduce(rstd[:, :], CW[:, :, :], AX.X, ALU.max))
            dve.tensor_tensor(CW[:, :, :], CW[:, :, :], rstd[:, :].unsqueeze(2).broadcast_to([P, NB, NE]), ALU.subtract).then_inc(gmax_ready, 1)
            dve.wait_ge(gexp_ready, 1)
            ch.link(dve.tensor_reduce(rstd[:, :], CW[:, :, :], AX.X, ALU.add))
            ch.link(dve.reciprocal(rstd[:, :], rstd[:, :]))
            ch.link(dve.tensor_tensor(CW[:, :, :], CW[:, :, :], rstd[:, :].unsqueeze(2).broadcast_to([P, NB, NE]), ALU.mult))
            others = CW[:, :, :].unsqueeze(2).broadcast_to([P, NB, NE, NE])
            own = CW[:, :, :].unsqueeze(3).broadcast_to([P, NB, NE, NE])
            ch.mark(dve.tensor_tensor(GT, others, own, ALU.is_gt))
            ch.link(dve.tensor_tensor(EQ, others, own, ALU.is_equal))
            ch.link(dve.tensor_tensor(EQ, EQ, LOW[:, :, :].unsqueeze(1).broadcast_to([P, NB, NE, NE]), ALU.mult))
            ch.link(dve.tensor_tensor(GT, GT, EQ, ALU.add))
            ch.link(dve.tensor_reduce(RK, GT, AX.X, ALU.add))
            dve.scalar_tensor_tensor(CW[:, :, :], RK, 2.0, CW[:, :, :], ALU.is_lt, ALU.mult).then_inc(cw_ready, 1)
            for c in range(len(CH)):
                dve.wait_ge(b2_ps, c + 1)
                o = (4 + 2 * (c % 2)) * 512
                xc = X[:, C0[c]:C0[c] + CH[c], :]
                dve.tensor_tensor(xc, xc, flat[:, o:o + CH[c] * D].rearrange("p (b n) -> p b n", n=D), ALU.add).then_inc(b2_taken, 1)
            dve.wait_ge(b2_taken, len(CH))
            cwf = CW[:, :, :].rearrange("p b e -> p (b e)")
            with dve.Fori(0, NE // 2) as i:
                ch.enter(i, 2 * (NB - len(CH)))
                add_experts(UN, i, X, lambda k, b: cwf[:, bass.ds(i * 2 + (k + b * NE), 1)])
                ch.leave(NE // 2)


_INS = ["x", "src", "dst", "L0_gnn_W1", "L0_gnn_b1", "L0_gnn_W2", "L0_gnn_b2", "L0_ffn_Wr", "L0_ffn_br", "L0_ffn_W1", "L0_ffn_b1",
        "L0_ffn_W2", "L0_ffn_b2", "L0_ffn_gamma", "L0_ffn_beta", "L1_gnn_W", "L1_gnn_att_src", "L1_gnn_att_dst", "L1_gnn_bias",
        "L1_ffn_gate_w", "L1_ffn_gate_b", "L1_ffn_W1", "L1_ffn_b1", "L1_ffn_W2", "L1_ffn_b2"]


def kernel(**inputs):
    import numpy as np
    import concourse.bacc as bacc
    from concourse.bass_utils import run_bass_kernel_spmd as run

    nc = bacc.Bacc("TRN2", target_bir_lowering=False, num_devices=1)
    arrays, aps = {}, {}
    for name in _INS:
        v = np.ascontiguousarray(inputs[name])
        arrays[f"{name}_dram"] = v
        aps[name] = nc.dram_tensor(f"{name}_dram", v.shape, mybir.dt.from_np(v.dtype), kind="ExternalInput").ap()
    out = nc.dram_tensor("out_dram", (N, D), F32, kind="ExternalOutput").ap()
    build(nc, aps, out)
    return run(nc, [arrays], core_ids=[0]).results[0]["out_dram"]
```
